# Optimizing a Trainium2 kernel written in Bass

```python
import numpy as np
import jax
import jax.numpy as jnp

def _softmax(x, axis=-1):
    return jax.nn.softmax(x, axis=axis)

def _gelu(x):
    return jax.nn.gelu(x, approximate=True)

def _silu(x):
    return jax.nn.silu(x)

def _sigmoid(x):
    return jax.nn.sigmoid(x)

def _layernorm(x, axis=-1, eps=1e-05):
    m = jnp.mean(x, axis=axis, keepdims=True)
    v = jnp.var(x, axis=axis, keepdims=True)
    return (x - m) / jnp.sqrt(v + eps)

def _scatter_add(tgt, idx, src, axis=0):
    return tgt.at[idx].add(src)

def _segment_sum(src, seg, n):
    return jax.ops.segment_sum(src, seg, n)
kernel_name = 'mk_macaron_d1_jaxref_r4_63acac'

def setup_inputs(seed: int=0):
    np.random.seed(seed)
    _w = jnp.asarray

    def _L0_attn_setup():
        import jax, jax.numpy as jnp
        import numpy as np
        B, L, D_IN, D_OUT, H, WIN = (1, 512, 256, 256, 16, 64)
        D_H = D_OUT // H
        key = jax.random.key(seed)
        ks = jax.random.split(key, 5)
        s = 0.02
        return {'x': jax.random.normal(ks[0], (B, L, D_IN), dtype=jnp.float32), 'Wq': jax.random.normal(ks[1], (D_IN, D_OUT), dtype=jnp.float32) * s, 'Wk': jax.random.normal(ks[2], (D_IN, D_OUT), dtype=jnp.float32) * s, 'Wv': jax.random.normal(ks[3], (D_IN, D_OUT), dtype=jnp.float32) * s, 'Wo': jax.random.normal(ks[4], (D_OUT, D_IN), dtype=jnp.float32) * s}
    _L0_attn_in = _L0_attn_setup()

    def _L0_ffn_setup():
        import jax, jax.numpy as jnp
        import numpy as np
        E = 8
        K = 2
        key = jax.random.key(seed)
        ks = jax.random.split(key, 8)
        B, T, d = (4, 512, 256)
        h = 4 * d // E
        s = 0.02
        X = jax.random.normal(ks[0], (B, T, d), jnp.float32)
        routing_W = jax.random.normal(ks[1], (E, d), jnp.float32) * s
        expert_bias = jnp.zeros((E,), jnp.float32)
        sW1 = jax.random.normal(ks[2], (d, h), jnp.float32) * s
        sb1 = jnp.zeros((h,), jnp.float32)
        sW2 = jax.random.normal(ks[3], (h, d), jnp.float32) * s
        sb2 = jnp.zeros((d,), jnp.float32)
        rW1 = jax.random.normal(ks[4], (E, d, h), jnp.float32) * s
        rb1 = jnp.zeros((E, h), jnp.float32)
        rW2 = jax.random.normal(ks[5], (E, h, d), jnp.float32) * s
        rb2 = jnp.zeros((E, d), jnp.float32)
        return dict(X=X, routing_W=routing_W, expert_bias=expert_bias, sW1=sW1, sb1=sb1, sW2=sW2, sb2=sb2, rW1=rW1, rb1=rb1, rW2=rW2, rb2=rb2)
    _L0_ffn_in = _L0_ffn_setup()
    _d = {'L0_attn_x': _L0_attn_in['x'], 'L0_attn_Wq': _L0_attn_in['Wq'], 'L0_attn_Wk': _L0_attn_in['Wk'], 'L0_attn_Wv': _L0_attn_in['Wv'], 'L0_attn_Wo': _L0_attn_in['Wo'], 'L0_ffn_routing_W': _L0_ffn_in['routing_W'], 'L0_ffn_expert_bias': _L0_ffn_in['expert_bias'], 'L0_ffn_sW1': _L0_ffn_in['sW1'], 'L0_ffn_sb1': _L0_ffn_in['sb1'], 'L0_ffn_sW2': _L0_ffn_in['sW2'], 'L0_ffn_sb2': _L0_ffn_in['sb2'], 'L0_ffn_rW1': _L0_ffn_in['rW1'], 'L0_ffn_rb1': _L0_ffn_in['rb1'], 'L0_ffn_rW2': _L0_ffn_in['rW2'], 'L0_ffn_rb2': _L0_ffn_in['rb2']}
    _x0 = _d['L0_attn_x']
    _d['L0_attn_x'] = jax.random.normal(jax.random.fold_in(jax.random.key(seed), 1), (16, 512, 256), dtype=_x0.dtype)
    del _x0
    return _d

def reference(L0_attn_x, L0_attn_Wq, L0_attn_Wk, L0_attn_Wv, L0_attn_Wo, L0_ffn_routing_W, L0_ffn_expert_bias, L0_ffn_sW1, L0_ffn_sb1, L0_ffn_sW2, L0_ffn_sb2, L0_ffn_rW1, L0_ffn_rb1, L0_ffn_rW2, L0_ffn_rb2):

    def _L0_attn_ref(x, Wq, Wk, Wv, Wo):
        import jax, jax.numpy as jnp
        import numpy as np
        B, L, D_IN, D_OUT, H, WIN = (1, 512, 256, 256, 16, 64)
        D_H = D_OUT // H
        Bx, Lx, _ = x.shape
        W = min(WIN, Lx)
        scale = D_H ** (-0.5)

        def split_heads(t):
            return t.reshape(Bx, Lx, H, D_H).transpose(0, 2, 1, 3)
        q = split_heads(x @ Wq)
        k = split_heads(x @ Wk)
        v = split_heads(x @ Wv)
        offsets = jnp.arange(W) - (W - 1)
        idx = jnp.arange(Lx)[:, None] + offsets[None, :]
        invalid = idx < 0
        idx = jnp.clip(idx, 0, Lx - 1)
        k_win = jnp.take(k, idx, axis=2)
        v_win = jnp.take(v, idx, axis=2)
        scores = jnp.einsum('bhld,bhlwd->bhlw', q, k_win) * scale
        scores = jnp.where(invalid[None, None, :, :], -jnp.inf, scores)
        attn = jax.nn.softmax(scores, axis=-1)
        ctx = jnp.einsum('bhlw,bhlwd->bhld', attn, v_win)
        ctx = ctx.transpose(0, 2, 1, 3).reshape(Bx, Lx, D_OUT)
        return ctx @ Wo

    def _L0_ffn_ref(X, routing_W, expert_bias, sW1, sb1, sW2, sb2, rW1, rb1, rW2, rb2):
        import jax, jax.numpy as jnp
        import numpy as np
        E = 8
        K = 2
        B, T, d = X.shape
        shared = jax.nn.silu(X @ sW1 + sb1) @ sW2 + sb2
        logits = jnp.einsum('btd,ed->bte', X, routing_W) + expert_bias
        activation = jnp.sqrt(jax.nn.softplus(logits))
        top_vals, top_idx = jax.lax.top_k(activation, K)
        combine = jnp.sum(jax.nn.one_hot(top_idx, E, dtype=X.dtype) * top_vals[..., None], axis=-2)
        Xf = X.reshape(-1, d)
        cf = combine.reshape(-1, E)
        hdn = jax.nn.silu(jnp.einsum('nd,edh->enh', Xf, rW1) + rb1[:, None, :])
        y = jnp.einsum('enh,ehd->end', hdn, rW2) + rb2[:, None, :]
        routed = jnp.einsum('ne,end->nd', cf, y).reshape(B, T, d)
        return shared + routed
    x = L0_attn_x
    x = x + 0.5 * _L0_ffn_ref(_layernorm(x, axis=-1), L0_ffn_routing_W, L0_ffn_expert_bias, L0_ffn_sW1, L0_ffn_sb1, L0_ffn_sW2, L0_ffn_sb2, L0_ffn_rW1, L0_ffn_rb1, L0_ffn_rW2, L0_ffn_rb2)
    x = x + _L0_attn_ref(_layernorm(x, axis=-1), L0_attn_Wq, L0_attn_Wk, L0_attn_Wv, L0_attn_Wo)
    x = x + 0.5 * _L0_ffn_ref(_layernorm(x, axis=-1), L0_ffn_routing_W, L0_ffn_expert_bias, L0_ffn_sW1, L0_ffn_sb1, L0_ffn_sW2, L0_ffn_sb2, L0_ffn_rW1, L0_ffn_rb1, L0_ffn_rW2, L0_ffn_rb2)
    return x

_drawn_inputs = setup_inputs


def setup_inputs(seed=0):
    import zlib

    import numpy as np

    out = dict(_drawn_inputs(seed))
    spreads = {'L0_ffn_expert_bias': (0.0, 0.1),
     'L0_ffn_sb1': (0.0, 0.666),
     'L0_ffn_sb2': (0.0, 0.1),
     'L0_ffn_rb1': (0.0, 0.462),
     'L0_ffn_rb2': (0.0, 0.1)}
    factors = {'L0_attn_Wq': 8.0, 'L0_attn_Wk': 8.0, 'L0_attn_Wv': 3.138, 'L0_attn_Wo': 3.139}
    for name, (base, spread) in spreads.items():
        noise = np.random.default_rng([zlib.crc32(name.encode()), seed]).standard_normal(out[name].shape)
        drawn = base * np.exp(spread * noise) if base else spread * noise
        out[name] = jnp.asarray(drawn.astype(out[name].dtype))
    for name, factor in factors.items():
        out[name] = (out[name] * factor).astype(out[name].dtype)
    return out
```

```python
import concourse.bass as bass
from concourse import mybir
from contextlib import ExitStack

F32 = mybir.dt.float32
F32R = mybir.dt.float32r
ALU = mybir.AluOpType
ACT = mybir.ActivationFunctionType
AX_X = mybir.AxisListType.X

P = 128
EPS = 1e-5
WIN = 64
NEG = -1e30

SLOT_A = ["E0", "T", "aN1", "E1", "aN2", "N1", "aX0", "aX1", "N2", "aQ0", "E2", "X0", "aV0", "X1", "aV1", "L",
          "aV2", "aV3", "aQ1", "E3", "J0", "J1", "E4", "R1", "J2", "J3", "E5", "J4", "E6", "J5", "R2", "J6", "J7",
          "E7", "E8", "C"]
SLOT_B = ["E0", "T", "J8", "E1", "E2", "K8", "J9", "J10", "J11", "E3", "J12", "J13", "J14", "J15", "J16", "J17",
          "J18", "E4", "aC", "E5", "aO", "aR", "N1", "N2", "E6", "X0", "X1", "L", "R1", "E7", "E8", "R2", "C"]
FRONT = ["N1", "N2", "X0", "X1", "L", "R1", "R2", "C"]
SLOT_FIRST = ["E0", "E1", "E2", "E3", "E4", "E5", "E6", "E7", "E8"]
FRONT_SECOND = ["aN1", "N1", "aN2", "N2", "aX0", "aX1", "X0", "X1", "L", "aQ0", "R1", "R2", "C",
                "aV0", "aV1", "aV2", "aV3", "aQ1"]
SLOT_SECOND = ["E0"] + [s for s in SLOT_A if s[0] == "J"] + SLOT_B[2:]
SLOT_LAST_BUT_ONE = [s for s in SLOT_A if s[0] in "EaJT"] + [s for s in SLOT_B if s[0] in "JK"] + ["aC"]
FRONT_LAST = ["aO", "aR"] + FRONT
SLOT_LAST = ["E0", "E1", "E2", "E3", "E4", "E5", "E6", "E7", "E8"]


def banks_of(slot):
    return [s for s in slot if s in ("X0", "X1", "L", "C") or s[0] == "E"]


def bank(order, step):
    return (order.index(step) + (len(order) == 4)) % 2


SERIES = [1.0 / q for q in (13, 11, 9, 7, 5, 3)]


def macaron_block(nc, x, wq, wk, wv, wo, routing_w, expert_bias, sw1, sb1, sw2, sb2, rw1, rb1, rw2, rb2, out,
                  gates_dram, qk_dram):
    B, L, D = x.shape
    E, _, HID = rw1.shape
    NE = E + 1
    KC = D // P
    NT = L // P
    H = 16
    DH = D // H
    HC = H // KC
    NP = HC // 2
    NW = L // WIN
    NJ = KC * NW
    SCALE = float(DH) ** -0.5
    assert HID == P and L == 512 and D == 256 and NP == 4

    with ExitStack() as ctx:
        def sb(name, shape, dt=F32):
            return ctx.enter_context(nc.sbuf_tensor(name, shape, dt))

        def ps(name, shape):
            return ctx.enter_context(nc.psum_tensor(name, shape, F32))

        def sem(name):
            return ctx.enter_context(nc.semaphore(name))

        w1h, w1l = sb("w1h", [P, NE, KC, P], F32R), sb("w1l", [P, NE, KC, P], F32R)
        w2h, w2l = sb("w2h", [P, NE, D], F32R), sb("w2l", [P, NE, D], F32R)
        wah, wal = sb("wah", [P, 4, KC, D], F32R), sb("wal", [P, 4, KC, D], F32R)
        rwh, rwl = sb("rwh", [P, KC, E], F32R), sb("rwl", [P, KC, E], F32R)
        rwf = sb("rwf", [P, KC, E])
        b2s = sb("b2s", [P, D], F32R)
        b1 = sb("b1", [P, NE])
        b1half = sb("b1half", [P, NE])
        ebias = sb("ebias", [P, E])
        ident = sb("ident", [P, P])
        mask = sb("mask", [P, 2, P])
        before = sb("before", [P, E, E])
        epsb = sb("epsb", [P, NT])
        spare, spare_pool = sb("spare", [P, 96]), sb("spare_pool", [P, 96])
        mhalf = sb("mhalf", [P, NT])
        phalf = sb("phalf", [P, NT * E])
        rowlo = sb("rowlo", [P, 2])
        xres = sb("xres", [P, 3, NT, D])
        xin, x1, x2 = xres[:, 0], xres[:, 1], xres[:, 2]
        stat, mv, rs = sb("stat", [P, NT, 6]), sb("mv", [P, NT, 2]), sb("rs", [P, NT])
        xn = sb("xn", [P, NT, D])
        xh, xl = sb("xh", [P, 2, KC, L], F32R), sb("xl", [P, 2, KC, L], F32R)
        lg = sb("lg", [P, NT, E])
        xn_flat = xn[:, :, :].rearrange("p t d -> p (t d)")
        gt = xn_flat[:, 0:NT * E * E].rearrange("p (t e j) -> p t e j", t=NT, e=E)
        eq = xn_flat[:, NT * E * E:2 * NT * E * E].rearrange("p (t e j) -> p t e j", t=NT, e=E)
        cfrow = xn_flat[0:E, 2 * NT * E * E:]
        rank, en, zz, zw, lp = (sb(n, [P, NT, E]) for n in ("rank", "en", "zz", "zw", "lp"))
        cfs = sb("cfs", [P, NT, P])
        cft = sb("cft", [P, 2, L], F32R)
        gate = sb("gate", [P, 4, L])
        tt, ag = sb("tt", [P, L]), sb("ag", [P, 2, L])
        gh, gl = sb("gh", [P, 2, L], F32R), sb("gl", [P, 2, L], F32R)
        stata, mva, rsa = sb("stata", [P, NT, 6]), sb("mva", [P, NT, 2]), sb("rsa", [P, NT])
        axh, axl = sb("axh", [P, KC, WIN + L], F32R), sb("axl", [P, KC, WIN + L], F32R)
        qkh, qkl = sb("qkh", [P, 2, L], F32R), sb("qkl", [P, 2, L], F32R)
        vh, vl = sb("vh", [P, NW, D], F32R), sb("vl", [P, NW, D], F32R)
        qs = sb("qs", [P, NP, NW, 2, WIN], F32R)
        ks = sb("ks", [P, NP, WIN + L], F32R)
        pr = sb("pr", [P, 3, NP, P])
        mx, rsum, rinv = sb("mx", [P, 3, NP]), sb("rsum", [P, 3, NP]), sb("rinv", [P, 3, NP])
        pth, ptl = sb("pth", [P, 2, L], F32R), sb("ptl", [P, 2, L], F32R)
        cd = sb("cd", [P, 2, HC, L // 2])
        cx = sb("cx", [P, L])
        b2f = cx[:, 0:D]
        xna = pr[:, 0:2].rearrange("p a r k -> p (a r k)").rearrange("p (t d) -> p t d", t=NT)
        hb = ps("hb", [P, 2, L])
        yb = ps("yb", [P, NT, D])
        sp_ = ps("sp_", [P, NP, 2 * P])
        ptb = ps("ptb", [P, L])
        cxb = ps("cxb", [P, L])
        ab = [ptb, cxb]

        w_raw, w_small, w_hi, w_lo, w_zero, w_const, w_mask, w_prep = (
            sem(n) for n in ("w_raw", "w_small", "w_hi", "w_lo", "w_zero", "w_const", "w_mask", "w_prep"))
        x_in, x_out = sem("x_in"), sem("x_out")
        f_stat, f_rstd, f_xn, f_xt, f_xh, f_xl = (
            sem(n) for n in ("f_stat", "f_rstd", "f_xn", "f_xt", "f_xh", "f_xl"))
        f_lg, f_rt, f_en, f_sq, f_cf, f_ct, f_cth, f_cr, f_g1 = (
            sem(n) for n in ("f_lg", "f_rt", "f_en", "f_sq", "f_cf", "f_ct", "f_cth", "f_cr", "f_g1"))
        f_gate = [sem("f_gate%d" % k) for k in range(4)]
        f_h, f_t, f_a, f_g, f_gh, f_gl, f_y, f_res = (
            sem(n) for n in ("f_h", "f_t", "f_a", "f_g", "f_gh", "f_gl", "f_y", "f_res"))
        a_stat, a_rstd, a_xn, a_xt, a_xh, a_xl, a_qk, a_qkh, a_qkl, a_v, a_vh, a_vl, a_stk, a_qw = (
            sem(n) for n in ("a_stat", "a_rstd", "a_xn", "a_xt", "a_xh", "a_xl", "a_qk", "a_qkh", "a_qkl",
                             "a_v", "a_vh", "a_vl", "a_stk", "a_qw"))
        a_s, a_m, a_p, a_ri, a_pn, a_pt, a_ph, a_pl, a_pv, a_ce, a_ch, a_cl, a_o, a_x2 = (
            sem(n) for n in ("a_s", "a_m", "a_p", "a_ri", "a_pn", "a_pt", "a_ph", "a_pl", "a_pv", "a_ce",
                             "a_ch", "a_cl", "a_o", "a_x2"))

        a_cx = [sem("a_cx%d" % k) for k in range(2)]

        NRANK = 7
        NRT = NRANK + 8 + len(SERIES)
        NSTK = 16 * 12
        NCX = 16 * 8

        def splits(p1, p2, pa):
            return [(p1[:, 0].rearrange("p k m -> p (k m)"), ag[:, 0, 0:KC * P]),
                    (p1[:, 1:NE].rearrange("p e k m -> p (e k m)"), cd[:, 0].rearrange("p h q -> p (h q)")),
                    (p2[:, 0, :], ag[:, 1, 0:D]),
                    (p2[:, 1:NE].rearrange("p e d -> p (e d)"), gate[:, :, :].rearrange("p g l -> p (g l)")),
                    (pa[:, 0:2].rearrange("p w k n -> p (w k n)"), x1.rearrange("p t d -> p (t d)")),
                    (pa[:, 2:4].rearrange("p w k n -> p (w k n)"), x2.rearrange("p t d -> p (t d)"))]

        NSPLIT = 6

        def wait(eng, s, value):
            if isinstance(value, int) and value <= 0:
                return
            eng.wait_ge(s, value)

        def before_step(b, k):
            return NJ * b + max(k, 0)

        def scored(step):
            return step != "J8" and int(step[1:]) < NJ

        sites = {}

        def apart(eng):
            k = sites[eng.engine] = sites.get(eng.engine, -1) + 1
            if eng.engine == nc.vector.engine:
                nc.vector.memset(spare[:, k:k + 1], 0.0)
            else:
                nc.gpsimd.tensor_tensor(spare_pool[:, k:k + 1], mhalf[:, 0:1], mhalf[:, 0:1], ALU.mult)

        def passes(eng, slot):
            slot(FRONT, -1, 1, None, None)
            slot(SLOT_FIRST, 0, 0, None, None)
            slot(["T"], 1, 1, 0, None)
            slot(FRONT_SECOND, 0, 0, 0, None)
            slot(SLOT_SECOND, 1, 1, 0, "L")
            with eng.Fori(1, B - 1) as i:
                slot(SLOT_A, i * 2, 0, i, "E8")
                slot(SLOT_B, i * 2 + 1, 1, i, "E8")
            slot(SLOT_LAST_BUT_ONE, 2 * B - 2, 0, B - 1, "E8")
            slot(["T"], 2 * B - 1, 1, None, None)
            slot(FRONT_LAST, 2 * B - 2, 0, B - 1, None)
            slot(SLOT_LAST, 2 * B - 1, 1, None, "L")
            slot(["T"], 2 * B, 0, None, None)

        block = ctx.enter_context(nc.Block())

        @block.sync
        def _(sp):
            sp.dma_start(xin, x[0].rearrange("(t p) d -> p t d", p=P)).then_inc(x_in, 16)
            sp.dma_start(ag[:, 0, 0:KC * P].rearrange("p (k m) -> p k m", k=KC),
                         sw1.rearrange("(k p) m -> p k m", p=P)).then_inc(w_raw, 16)
            for e in range(E):
                sp.dma_start(cd[:, 0, e, :].rearrange("p (k m) -> p k m", k=KC),
                             rw1[e].rearrange("(k p) m -> p k m", p=P)).then_inc(w_raw, 16)
            sp.dma_start(ag[:, 1, 0:D], sw2).then_inc(w_raw, 16)
            sp.dma_start(gate[:, :, :].rearrange("p a (b d) -> p (a b) d", d=D),
                         rw2.rearrange("e h d -> h e d")).then_inc(w_raw, 16)
            for s, w in enumerate((wq, wk, wv, wo)):
                sp.dma_start(xres[:, 1 + s // 2, 2 * (s % 2):2 * (s % 2) + 2, :],
                             w.rearrange("(k p) n -> p k n", p=P)).then_inc(w_raw, 16)

            def rows(a, row):
                return a[bass.ds(row, 1)].rearrange("a (t p) d -> p (a t) d", p=P)

            def spread(m):
                sp.dma_start(gate[:, m % 4, :], gates_dram[m].partition_broadcast(P)).then_inc(f_gate[m % 4], 16)

            def stack(c):
                for part in range(4):
                    qt, kt = qk_dram[c, 0, part % 2], qk_dram[c, 1, part // 2]
                    sp.dma_start(ks[32 * part:32 * part + 32, :, WIN:WIN + L].bitcast(F32), kt).then_inc(a_stk, 16)
                    for hd in range(2):
                        lo = 32 * part + DH * hd
                        sp.dma_start(qs[lo:lo + DH, :, :, hd, :].bitcast(F32),
                                     qt[DH * hd:DH * hd + DH].rearrange("p r (w q) -> p (r w) q", w=NW)).then_inc(a_stk, 16)

            def slot(steps, n, par, b, prev):
                for s in steps:
                    if s == "T":
                        src = 1 - par
                        last_pass = isinstance(n, int) and n == 2 * B
                        first_pass = isinstance(n, int) and n == 1
                        if last_pass or (src == 0 and not first_pass):
                            row = B - 1 if last_pass else (B - 2 if b is None else b - 1)
                            sp.wait_ge(f_res, 2 * n)
                            sp.dma_start(rows(out, row), x2).then_inc(x_out, 16)
                        else:
                            row = 1 if first_pass else b + 1
                            if isinstance(row, int) and row >= B:
                                continue
                            sp.wait_ge(f_res, 2 * n)
                            sp.dma_start(xin, rows(x, row)).then_inc(x_in, 16)
                    elif s == "C":
                        sp.wait_ge(f_cr, n + 2)
                        sp.dma_start(gates_dram[:, :], cfrow).then_inc(f_g1, 16)
                        sp.wait_ge(f_g1, 16 * n + 32)
                        for m in range(4):
                            spread(m)
                    elif s[0] == "E":
                        e = int(s[1])
                        if 1 <= e <= 4:
                            sp.wait_ge(f_a, NE * n + e + 1)
                            spread(e + 3)
                    elif s in ("aQ0", "aQ1"):
                        c = int(s[2])
                        sp.wait_ge(a_qkl, 4 * b + 2 * c + 2)
                        for hl, t in enumerate((qkh, qkl)):
                            for u in range(2):
                                sp.dma_start(qk_dram[c, u, hl].rearrange("p r l -> r p l"),
                                             t[:, u, :].bitcast(F32)).then_inc(a_qw, 16)
                        if c == 0:
                            sp.wait_ge(a_qw, 128 * b + 64)
                            stack(0)
                    elif s == "J8":
                        sp.wait_ge(a_s, NJ * b + NW)
                        stack(1)
                    if s[0] == "J":
                        j = int(s[1:]) - 3
                        if j >= 0 and j % 4 == 3:
                            c, hf = j // NW, (j % NW) // 4
                            sp.wait_ge(a_ce, NJ * b + j + 1)
                            if hf == 0:
                                wait(sp, a_cl, 2 * b + c)
                            for h in range(HC):
                                sp.dma_start(cx[DH * h:DH * h + DH, hf * (L // 2):(hf + 1) * (L // 2)],
                                             cd[DH * h:DH * h + DH, hf, h, :]).then_inc(a_cx[hf], 16)

            passes(sp, slot)
            sp.wait_ge(x_out, 16 * B)

        @block.gpsimd
        def _(pool):
            nc.gpsimd.memset(ident[:], 0.0).then_inc(w_const, 1)
            nc.gpsimd.memset(mask[:], 0.0).then_inc(w_const, 1)
            nc.gpsimd.memset(before[:], 1.0).then_inc(w_const, 1)
            nc.gpsimd.memset(rowlo[:], 1.0).then_inc(w_const, 1)
            nc.gpsimd.memset(mhalf[:], -0.5).then_inc(w_const, 1)
            nc.gpsimd.memset(phalf[:], 0.5).then_inc(w_const, 1)
            nc.gpsimd.memset(epsb[:], EPS).then_inc(w_const, 1)
            pool.wait_ge(w_const, 7)

            def select(at, cmp, fill, base, pattern, mult, done):
                nc.gpsimd.affine_select(out=at, in_=at, compare_op=cmp, fill=fill, base=base, pattern=pattern,
                                        channel_multiplier=mult).then_inc(w_const, 1)
                pool.wait_ge(w_const, done)
            select(ident[:], ALU.not_equal, 1.0, 0, [[-1, P]], 1, 8)
            for m in range(2):
                select(mask[0:WIN, m, :], ALU.is_ge, NEG, -1, [[1, P]], -1, 9 + 2 * m)
                select(mask[0:WIN, m, :], ALU.is_ge, NEG, WIN, [[-1, P]], 1, 10 + 2 * m)
            select(mask[0:WIN, 0, :], ALU.is_ge, NEG, -WIN, [[1, P]], 0, 13)
            select(before[:], ALU.is_gt, 0.0, 0, [[1, E], [-1, E]], 0, 14)
            select(rowlo[:, 0:1], ALU.is_ge, 0.0, -48, [[0, 1]], 1, 15)
            select(rowlo[:, 0:1], ALU.is_ge, 0.0, 57, [[0, 1]], -1, 16)
            select(rowlo[:, 0:1], ALU.not_equal, 0.0, -56, [[0, 1]], 1, 17)
            pool.dma_start(mask[WIN:2 * WIN, :, :], mask[0:WIN, :, :]).then_inc(w_mask, 16)
            pool.wait_ge(w_mask, 16)

            def slot(steps, n, par, b, prev):
                for s in steps:
                    if s == "N1":
                        m = n + 1
                        pool.wait_ge(f_stat, 8 * m + 8)
                        wait(pool, f_xn, 4 * m)
                        nc.gpsimd.tensor_tensor(rs[:], mv[:, :, 1], epsb[:], ALU.add).then_inc(f_rstd, 1)
                        pool.wait_ge(f_rstd, 2 * m + 1)
                        nc.gpsimd.tensor_tensor(rs[:], rs[:], mhalf[:], ALU.pow).then_inc(f_rstd, 1)
                    elif s == "aN1":
                        pool.wait_ge(a_stat, 8 * b + 8)
                        wait(pool, a_xn, 4 * b)
                        nc.gpsimd.tensor_tensor(rsa[:], mva[:, :, 1], epsb[:], ALU.add).then_inc(a_rstd, 1)
                        pool.wait_ge(a_rstd, 2 * b + 1)
                        nc.gpsimd.tensor_tensor(rsa[:], rsa[:], mhalf[:], ALU.pow).then_inc(a_rstd, 1)
                    elif s == "R1":
                        m = n + 1
                        pool.wait_ge(f_rt, NRT * m + NRT)
                        wait(pool, f_cf, 4 * m)
                        lp2 = lp[:, :, :].rearrange("p t e -> p (t e)")
                        nc.gpsimd.tensor_tensor(zz[:, :, :].rearrange("p t e -> p (t e)"), lp2, phalf[:],
                                                ALU.pow).then_inc(f_sq, 1)
                    elif s[0] == "E":
                        e = int(s[1])
                        pool.wait_ge(f_gh, NE * n + e + 1)
                        wait(pool, f_y, NE * n + e - 1)
                        nc.gpsimd.tensor_tensor(gl[:, (e + par) % 2, :], ag[:, (e + par) % 2, :], gh[:, (e + par) % 2, :].bitcast(F32),
                                                ALU.subtract).then_inc(f_gl, 1)
                    elif s[0] == "J" and 1 <= int(s[1:]) <= NJ:
                        j = int(s[1:]) - 1
                        pool.wait_ge(a_ri, NJ * b + j + 1)
                        nc.gpsimd.tensor_tensor(pr[:, j % 3], pr[:, j % 3],
                                                rinv[:, j % 3, :].unsqueeze(2).to_broadcast([P, NP, P]),
                                                ALU.mult).then_inc(a_pn, 1)
                        if j == NW + 3:
                            split_context(b, 0)
                    elif s == "aC":
                        split_context(b, 1)

            def split_context(b, c):
                pool.wait_ge(a_ch, 2 * b + c + 1)
                nc.gpsimd.tensor_tensor(axl[:, c, WIN:WIN + L], cx[:], axh[:, c, WIN:WIN + L].bitcast(F32),
                                        ALU.subtract).then_inc(a_cl, 1)

            passes(pool, slot)

        @block.scalar
        def _(act):
            act.dma_start(b1[:, 0:1], sb1.rearrange("(p a) -> p a", a=1)).then_inc(w_small, 16)
            act.dma_start(b1[:, 1:NE], rb1.rearrange("e p -> p e"), allow_slow_non_contiguous=True).then_inc(w_small, 16)
            act.dma_start(ebias[:], expert_bias.rearrange("(a e) -> a e", a=1).partition_broadcast(P),
                          allow_slow_non_contiguous=True).then_inc(w_small, 16)
            for k in range(KC):
                act.dma_start(rwf[:, k, :], routing_w[:, k * P:(k + 1) * P].rearrange("e p -> p e"),
                              allow_slow_non_contiguous=True) \
                    .then_inc(w_small, 16)
            act.wait_ge(w_zero, 2)
            for r in (32, 40, 48):
                act.dma_start(b2f[r:r + E, :], rb2).then_inc(w_small, 16)
            for r in (56, 57):
                act.dma_start(b2f[r:r + 1, :], sb2.rearrange("(a d) -> a d", a=1)).then_inc(w_small, 16)
            act.wait_ge(w_raw, 16 * (E + 7))
            for dst, src in splits(w1h, w2h, wah):
                nc.scalar.activation(dst, src, ACT.Copy).then_inc(w_hi, 1)
            act.wait_ge(w_small, 16 * 10)
            nc.scalar.activation(rwh[:], rwf[:], ACT.Copy).then_inc(w_hi, 1)

            def slot(steps, n, par, b, prev):
                order = banks_of(steps)
                for s in steps:
                    if s in ("X0", "X1"):
                        c, m, q = int(s[1]), n + 1, 1 - par
                        act.wait_ge(f_xt, 2 * m + c + 1)
                        wait(act, f_h, NE * n)
                        nc.scalar.activation(xh[:, q, c, :], hb[:, bank(order, s), :], ACT.Copy).then_inc(f_xh, 1)
                    elif s == "L":
                        act.wait_ge(f_rt, NRT * (n + 1) + 2)
                        nc.scalar.activation(en[:], en[:], ACT.Exp).then_inc(f_en, 1)
                    elif s == "C":
                        act.wait_ge(f_cr, n + 2)
                        wait(act, f_y, NE * n)
                        nc.scalar.activation(cft[:, 1 - par, :], hb[:, bank(order, s), :], ACT.Copy).then_inc(f_cth, 1)
                    elif s[0] == "E":
                        e = int(s[1])
                        k = (e + par) % 2
                        act.wait_ge(f_h, NE * n + e + 1)
                        wait(act, f_g, NE * n + e)
                        nc.scalar.activation(tt[:], hb[:, bank(order, s), :], ACT.Tanh, bias=b1half[:, e:e + 1],
                                             scale=0.5).then_inc(f_t, 1)
                        act.wait_ge(f_g, NE * n + e + 1)
                        wait(act, f_y, NE * n + e - 1)
                        nc.scalar.activation(gh[:, k, :], ag[:, k, :], ACT.Copy).then_inc(f_gh, 1)
                    elif s in ("aX0", "aX1"):
                        c = int(s[2])
                        act.wait_ge(a_xt, 2 * b + c + 1)
                        wait(act, a_o, b)
                        nc.scalar.activation(axh[:, c, WIN:WIN + L], ab[c][:], ACT.Copy).then_inc(a_xh, 1)
                    elif s in ("aQ0", "aQ1"):
                        for u in range(2):
                            k = 2 * int(s[2]) + u
                            act.wait_ge(a_qk, 4 * b + k + 1)
                            wait(act, a_qw, 64 * (2 * b + int(s[2])))
                            nc.scalar.activation(qkh[:, u, :], ab[u][:], ACT.Copy).then_inc(a_qkh, 1)
                    elif s[:2] == "aV":
                        u = int(s[2])
                        act.wait_ge(a_v, 4 * b + u + 1)
                        wait(act, a_pv, NJ * b)
                        nc.scalar.activation(vh[:, 2 * u:2 * u + 2, :],
                                             ab[u % 2][:].rearrange("p (w d) -> p w d", w=2),
                                             ACT.Copy).then_inc(a_vh, 1)
                    elif s[0] in "JK":
                        st = int(s[1:])
                        if scored(s):
                            j = st
                            for r in range(NP):
                                act.wait_ge(a_m, 4 * (NJ * b + j) + r + 1)
                                if r == 0:
                                    wait(act, a_ri, before_step(b, j - 2))
                                nc.scalar.activation(pr[:, j % 3, r, :], pr[:, j % 3, r, :], ACT.Exp,
                                                     bias=mx[:, j % 3, r:r + 1], scale=-1.0,
                                                     accum_out=rsum[:, j % 3, r:r + 1]).then_inc(a_p, 1)
                        if s[0] == "J" and 2 <= st <= NJ + 1:
                            j = st - 2
                            act.wait_ge(a_pt, NJ * b + j + 1)
                            wait(act, a_pv, NJ * b + j - 1)
                            nc.scalar.activation(pth[:, j % 2, :], ptb[:], ACT.Copy).then_inc(a_ph, 1)
                        if s[0] == "J" and 3 <= st <= NJ + 2:
                            j = st - 3
                            hf = j // 4 % 2
                            act.wait_ge(a_pv, NJ * b + j + 1)
                            if j % 4 == 0:
                                wait(act, a_cx[hf], NCX * (2 * b + j // NW))
                            nc.scalar.activation(cd[:, hf, :, (j % 4) * WIN:(j % 4 + 1) * WIN],
                                                 cxb[:].rearrange("p (h q) -> p h q", h=HC),
                                                 ACT.Copy).then_inc(a_ce, 1)

            passes(act, slot)

        @block.vector
        def _(dve):
            nc.vector.memset(b2f, 0.0).then_inc(w_zero, 1)
            nc.vector.memset(cfs[:], 0.0).then_inc(w_zero, 1)
            nc.vector.memset(qs[:].bitcast(F32), 0.0).then_inc(w_zero, 1)
            nc.vector.memset(ks[:, :, 0:WIN].bitcast(F32), 0.0).then_inc(w_zero, 1)
            nc.vector.memset(axh[:, :, 0:WIN].bitcast(F32), 0.0).then_inc(w_zero, 1)
            nc.vector.memset(axl[:, :, 0:WIN].bitcast(F32), 0.0).then_inc(w_zero, 1)
            dve.wait_ge(w_zero, 2)
            nc.vector.memset(cfs[:, :, 56:58], 1.0).then_inc(w_zero, 1)
            for k, ((dst, src), (hi, _)) in enumerate(zip(splits(w1l, w2l, wal), splits(w1h, w2h, wah))):
                dve.wait_ge(w_hi, k + 1)
                nc.vector.tensor_tensor(dst, src, hi.bitcast(F32), ALU.subtract).then_inc(w_lo, 1)
            dve.wait_ge(w_hi, NSPLIT + 1)
            nc.vector.tensor_tensor(rwl[:], rwf[:], rwh[:].bitcast(F32), ALU.subtract).then_inc(w_lo, 1)
            dve.wait_ge(w_small, 16 * 10)
            nc.vector.tensor_scalar(b1half[:], b1[:], 0.5, None, ALU.mult).then_inc(w_lo, 1)
            dve.wait_ge(w_const, 17)
            b2h = b2s
            nc.vector.tensor_scalar(rowlo[:, 1:2], rowlo[:, 0:1], -1.0, 1.0, ALU.mult, ALU.add).then_inc(w_prep, 1)
            nc.vector.tensor_scalar(b2f, b2f, 2.0, None, ALU.mult).then_inc(w_prep, 1)
            dve.wait_ge(w_prep, 2)
            nc.vector.tensor_copy(b2h[:], b2f).then_inc(w_prep, 1)
            dve.wait_ge(w_prep, 3)
            nc.vector.tensor_tensor(b2f, b2f, b2h[:].bitcast(F32), ALU.subtract).then_inc(w_prep, 1)
            dve.wait_ge(w_prep, 4)
            nc.vector.tensor_scalar(b2f, b2f, rowlo[:, 0:1], None, ALU.mult).then_inc(w_prep, 1)
            dve.wait_ge(w_prep, 5)
            nc.vector.scalar_tensor_tensor(b2s[:], b2s[:].bitcast(F32), rowlo[:, 1:2], b2f, ALU.mult, ALU.add) \
                .then_inc(w_prep, 1)
            dve.wait_ge(w_mask, 16)
            dve.wait_ge(w_zero, 7)

            def stats(src, st, out_mv, s, done):
                for t in range(NT):
                    nc.vector.bn_stats(st[:, t, :], src[:, t, :]).then_inc(s, 1)
                dve.wait_ge(s, done + 4)
                apart(dve)
                for t in range(NT):
                    nc.vector.bn_aggr(out_mv[:, t, :], st[:, t, :]).then_inc(s, 1)

            def routing(n, psum):
                at = [0]

                def op(ins):
                    at[0] += 1
                    ins.then_inc(f_rt, 1)
                    dve.wait_ge(f_rt, NRT * n + at[0])
                dve.wait_ge(f_lg, n + 1)
                wait(dve, f_cf, 4 * n)
                op(nc.vector.tensor_tensor(lg[:], psum[:, 0:NT * E].rearrange("p (t e) -> p t e", t=NT),
                                           ebias[:].unsqueeze(1).to_broadcast([P, NT, E]), ALU.add))
                op(nc.vector.scalar_tensor_tensor(en[:], lg[:], -1.0, lg[:], ALU.mult, ALU.min))
                lj = lg[:].unsqueeze(2).to_broadcast([P, NT, E, E])
                le = lg[:].unsqueeze(3).to_broadcast([P, NT, E, E])
                op(nc.vector.tensor_tensor(gt, lj, le, ALU.is_gt))
                op(nc.vector.tensor_tensor(eq, lj, le, ALU.is_equal))
                op(nc.vector.tensor_tensor(eq, eq, before[:].unsqueeze(1).to_broadcast([P, NT, E, E]),
                                           ALU.mult))
                op(nc.vector.tensor_tensor(gt, gt, eq, ALU.add))
                op(nc.vector.tensor_reduce(rank[:], gt, AX_X, ALU.add))
                assert at[0] == NRANK

            def softplus(n):
                at = [NRANK]

                def op(ins):
                    at[0] += 1
                    ins.then_inc(f_rt, 1)
                    dve.wait_ge(f_rt, NRT * n + at[0])
                dve.wait_ge(f_en, n + 1)
                wait(dve, f_sq, n)
                op(nc.vector.tensor_scalar(zw[:], en[:], 2.0, None, ALU.add))
                op(nc.vector.reciprocal(zw[:], zw[:]))
                op(nc.vector.tensor_tensor(en[:], en[:], zw[:], ALU.mult))
                op(nc.vector.tensor_tensor(zw[:], en[:], en[:], ALU.mult))
                op(nc.vector.tensor_scalar(lp[:], zw[:], 1.0 / 15, None, ALU.mult))
                for q in SERIES:
                    op(nc.vector.scalar_tensor_tensor(lp[:], lp[:], q, zw[:], ALU.add, ALU.mult))
                op(nc.vector.scalar_tensor_tensor(lp[:], lp[:], 1.0, en[:], ALU.add, ALU.mult))
                op(nc.vector.tensor_scalar(lp[:], lp[:], 2.0, None, ALU.mult))
                op(nc.vector.scalar_tensor_tensor(lp[:], lg[:], 0.0, lp[:], ALU.max, ALU.add))
                assert at[0] == NRT

            def slot(steps, n, par, b, prev):
                order = banks_of(steps)
                for s in steps:
                    step(s, order, n, par, b)

            def step(s, order, n, par, b):
                m, q = n + 1, 1 - par
                src = xin if (q == 1 or (isinstance(m, int) and m == 0)) else x2
                if isinstance(m, int) and m == 2 * B - 1:
                    src = x2
                if s == "N1":
                    if src is xin:
                        row = 0 if (isinstance(m, int) and m == 0) else (1 if isinstance(m, int) else b + 1)
                        dve.wait_ge(x_in, 16 * row + 16)
                    else:
                        dve.wait_ge(a_x2, 2 * b + 2)
                    wait(dve, f_rstd, 2 * m)
                    wait(dve, f_xn, 4 * m)
                    stats(src, stat, mv, f_stat, 8 * m)
                elif s == "N2":
                    dve.wait_ge(f_rstd, 2 * m + 2)
                    wait(dve, f_xt, 2 * m)
                    for t in range(NT):
                        nc.vector.tensor_scalar(xn[:, t, :], src[:, t, :], mv[:, t, 0:1], rs[:, t:t + 1],
                                                ALU.subtract, ALU.mult).then_inc(f_xn, 1)
                elif s in ("X0", "X1"):
                    c = int(s[1])
                    dve.wait_ge(f_xh, 2 * m + c + 1)
                    nc.vector.tensor_tensor(xl[:, q, c, :], hb[:, bank(order, s), :], xh[:, q, c, :].bitcast(F32),
                                            ALU.subtract).then_inc(f_xl, 1)
                elif s == "L":
                    routing(m, hb[:, bank(order, s), :])
                elif s == "R1":
                    softplus(m)
                elif s == "R2":
                    dve.wait_ge(f_sq, m + 1)
                    wait(dve, f_ct, m)
                    nc.vector.scalar_tensor_tensor(cfs[:, :, 0:E], rank[:], 2.0, zz[:], ALU.is_lt, ALU.mult) \
                        .then_inc(f_cf, 1)
                    dve.wait_ge(f_cf, 4 * m + 1)
                    nc.vector.tensor_copy(cfs[:, :, 32:32 + E].bitcast(F32R), cfs[:, :, 0:E]).then_inc(f_cf, 1)
                    nc.vector.tensor_copy(cfs[:, :, 48:48 + E].bitcast(F32R), cfs[:, :, 0:E]).then_inc(f_cf, 1)
                    dve.wait_ge(f_cf, 4 * m + 3)
                    nc.vector.tensor_tensor(cfs[:, :, 40:40 + E], cfs[:, :, 0:E], cfs[:, :, 32:32 + E],
                                            ALU.subtract).then_inc(f_cf, 1)
                elif s == "C":
                    dve.wait_ge(f_ct, m + 1)
                    nc.vector.tensor_copy(cfrow, hb[0:E, bank(order, s), :]).then_inc(f_cr, 1)
                elif s[0] == "E":
                    e = int(s[1])
                    k = (e + par) % 2
                    dve.wait_ge(f_t, NE * n + e + 1)
                    wait(dve, f_gl, NE * n + e - 1)
                    if e == 0:
                        nc.vector.tensor_scalar(ag[:, k, :], hb[:, bank(order, s), :], b1[:, 0:1], None, ALU.add) \
                            .then_inc(f_a, 1)
                    else:
                        g = (e - 1) % 4
                        dve.wait_ge(f_gate[g], 32 * n + 16 * ((e - 1) // 4) + 16)
                        nc.vector.scalar_tensor_tensor(ag[:, k, :], hb[:, bank(order, s), :], b1[:, e:e + 1],
                                                       gate[:, g, :], ALU.add, ALU.mult).then_inc(f_a, 1)
                    dve.wait_ge(f_a, NE * n + e + 1)
                    nc.vector.scalar_tensor_tensor(ag[:, k, :], tt[:], 1.0, ag[:, k, :], ALU.add, ALU.mult) \
                        .then_inc(f_g, 1)
                elif s == "T":
                    p1 = n - 1
                    first = isinstance(p1, int) and p1 == 0
                    last = isinstance(p1, int) and p1 == 2 * B - 1
                    odd = (par == 0)
                    into_x1 = first or (odd and not last)
                    rd, wr = (xin, x1) if into_x1 else (x2, x2)
                    dve.wait_ge(f_y, NE * n)
                    if into_x1 and b is not None:
                        wait(dve, a_x2, 2 * b)
                    for u in range(2):
                        nc.vector.scalar_tensor_tensor(
                            wr[:, 2 * u:2 * u + 2, :], yb[:, 2 * u:2 * u + 2, :], 0.25, rd[:, 2 * u:2 * u + 2, :],
                            ALU.mult, ALU.add).then_inc(f_res, 1)
                elif s == "aN1":
                    dve.wait_ge(f_res, 2 if isinstance(b, int) and b == 0 else 4 * b)
                    wait(dve, a_rstd, 2 * b)
                    wait(dve, a_xn, 4 * b)
                    stats(x1, stata, mva, a_stat, 8 * b)
                elif s == "aN2":
                    dve.wait_ge(a_rstd, 2 * b + 2)
                    wait(dve, a_pt, NJ * b)
                    for t in range(NT):
                        nc.vector.tensor_scalar(xna[:, t, :], x1[:, t, :], mva[:, t, 0:1], rsa[:, t:t + 1],
                                                ALU.subtract, ALU.mult).then_inc(a_xn, 1)
                elif s in ("aX0", "aX1"):
                    c = int(s[2])
                    dve.wait_ge(a_xh, 2 * b + c + 1)
                    nc.vector.tensor_tensor(axl[:, c, WIN:WIN + L], ab[c][:], axh[:, c, WIN:WIN + L].bitcast(F32),
                                            ALU.subtract).then_inc(a_xl, 1)
                elif s in ("aQ0", "aQ1"):
                    for u in range(2):
                        dve.wait_ge(a_qkh, 4 * b + 2 * int(s[2]) + u + 1)
                        nc.vector.tensor_tensor(qkl[:, u, :], ab[u][:], qkh[:, u, :].bitcast(F32),
                                                ALU.subtract).then_inc(a_qkl, 1)
                elif s[:2] == "aV":
                    u = int(s[2])
                    dve.wait_ge(a_vh, 4 * b + u + 1)
                    nc.vector.tensor_tensor(vl[:, 2 * u:2 * u + 2, :], ab[u % 2][:].rearrange("p (w d) -> p w d", w=2),
                                            vh[:, 2 * u:2 * u + 2, :].bitcast(F32), ALU.subtract).then_inc(a_vl, 1)
                elif s == "aC":
                    high_context(b, 1)
                elif s == "aR":
                    dve.wait_ge(a_o, b + 1)
                    wait(dve, x_out, 16 * b)
                    for u in range(2):
                        nc.vector.tensor_tensor(x2[:, 2 * u:2 * u + 2, :], sp_[:, 2 * u:2 * u + 2, :],
                                                x1[:, 2 * u:2 * u + 2, :], ALU.add).then_inc(a_x2, 1)
                elif s[0] in "JK":
                    st = int(s[1:])
                    if s[0] == "J" and 1 <= st <= NJ:
                        j = st - 1
                        dve.wait_ge(a_p, 4 * (NJ * b + j) + 4)
                        wait(dve, a_pn, before_step(b, j - 2))
                        nc.vector.reciprocal(rinv[:, j % 3, :], rsum[:, j % 3, :]).then_inc(a_ri, 1)
                    if scored(s):
                        j, w = st, st % NW
                        off = WIN * w - min(WIN * w, WIN + L - 2 * P)
                        dve.wait_ge(a_s, NJ * b + j + 1)
                        wait(dve, a_pt, before_step(b, j - 2))
                        wait(dve, a_p, before_step(b, j - 2) * 4)
                        apart(dve)
                        for r in range(NP):
                            nc.vector.tensor_tensor_reduce(
                                out=pr[:, j % 3, r, :], in0=sp_[:, r, off:off + P], in1=mask[:, min(w, 1), :],
                                scale=-SCALE, scalar=3e38, op0=ALU.add, op1=ALU.min,
                                accum_out=mx[:, j % 3, r:r + 1]).then_inc(a_m, 1)
                    if s[0] == "J" and 2 <= st <= NJ + 1:
                        j = st - 2
                        dve.wait_ge(a_ph, NJ * b + j + 1)
                        nc.vector.tensor_tensor(ptl[:, j % 2, :], ptb[:], pth[:, j % 2, :].bitcast(F32),
                                                ALU.subtract).then_inc(a_pl, 1)
                    if st == NW + 4:
                        high_context(b, 0)

            def high_context(b, c):
                for hf in range(2):
                    dve.wait_ge(a_cx[hf], NCX * (2 * b + c + 1))
                wait(dve, a_qk, 4 * b + 4)
                nc.vector.tensor_copy(axh[:, c, WIN:WIN + L], cx[:]).then_inc(a_ch, 1)

            passes(dve, slot)

        @block.tensor
        def _(pe):
            pe.wait_ge(w_const, 17)
            pe.wait_ge(w_lo, NSPLIT + 2)
            pe.wait_ge(w_prep, 6)
            pe.wait_ge(w_zero, 7)

            def freed(step, m, prv_par):
                if step[0] == "X":
                    wait(pe, f_xl, 2 * m + int(step[1]) + 1)
                elif step == "L":
                    wait(pe, f_rt, NRT * m + 1)
                elif step == "C":
                    wait(pe, f_cth, m + 1)
                else:
                    wait(pe, f_a, NE * m + int(step[1]) + 1)

            def take_bank(order, s, n, prev):
                p = order.index(s)
                if len(order) == 4:
                    if p >= 2:
                        freed(order[p - 2], n + 1, 0)
                    else:
                        freed(("E7", "E8")[p], n, 0)
                elif p >= 2:
                    before_ = order[p - 2]
                    freed(before_, n if before_[0] == "E" else n + 1, 0)
                elif p == 0:
                    freed("C", n, 0)
                else:
                    freed(prev or "L", n - 1 if (prev or "L")[0] == "E" else n, 0)

            def three(dst, ah, al, bh, bl, start, stop, **kw):
                nc.tensor.matmul(dst, ah, bh, start=start, stop=False, **kw)
                nc.tensor.matmul(dst, al, bh, start=False, stop=False, **kw)
                return nc.tensor.matmul(dst, ah, bl, start=False, stop=stop, **kw)

            def second(n, e, par):
                k = (e + par) % 2
                pe.wait_ge(f_gh, NE * n + e + 1)
                pe.wait_ge(f_gl, NE * n + e + 1)
                if e == 0:
                    wait(pe, f_res, 2 * n)
                for t in range(NT):
                    mm = three(yb[:, t, :], gh[:, k, t * P:(t + 1) * P], gl[:, k, t * P:(t + 1) * P],
                               w2h[:, e, :], w2l[:, e, :], start=(e == 0 and t % 2 == 0), stop=False,
                               skip_group_check=True)
                if e < NE - 1:
                    mm.then_inc(f_y, 1)
                else:
                    pe.wait_ge(f_cth, n + 1)
                    for t in range(NT):
                        mm = nc.tensor.matmul(yb[:, t, :], cft[:, par, t * P:(t + 1) * P], b2s[:], start=False, stop=True,
                                              skip_group_check=True)
                    mm.then_inc(f_y, 1)

            def slot(steps, n, par, b, prev):
                order = banks_of(steps)
                for s in steps:
                    m, q = n + 1, 1 - par
                    if s in order:
                        take_bank(order, s, n, prev)
                        hbk = hb[:, bank(order, s), :]
                    if s in ("X0", "X1"):
                        c = int(s[1])
                        pe.wait_ge(f_xn, 4 * m + 4)
                        for t in range(NT):
                            mm = nc.tensor.transpose(hbk[:, t * P:(t + 1) * P], xn[:, t, c * P:(c + 1) * P], ident[:])
                        mm.then_inc(f_xt, 1)
                    elif s == "L":
                        pe.wait_ge(f_xl, 2 * m + 2)
                        for t in range(NT):
                            ts = slice(t * P, (t + 1) * P)
                            for k in range(KC):
                                mm = three(hbk[:, t * E:(t + 1) * E], xh[:, q, k, ts], xl[:, q, k, ts],
                                           rwh[:, k, :], rwl[:, k, :], start=(k == 0), stop=(k == KC - 1))
                        mm.then_inc(f_lg, 1)
                    elif s == "C":
                        pe.wait_ge(f_cf, 4 * m + 4)
                        for t in range(NT):
                            mm = nc.tensor.transpose(hbk[:, t * P:(t + 1) * P], cfs[:, t, :], ident[:])
                        mm.then_inc(f_ct, 1)
                    elif s[0] == "E":
                        e = int(s[1])
                        if e == 0:
                            pe.wait_ge(f_xl, 2 * n + 2)
                        for k in range(KC):
                            mm = three(hbk, w1h[:, e, k, :], w1l[:, e, k, :], xh[:, par, k, :], xl[:, par, k, :],
                                       start=(k == 0), stop=(k == KC - 1))
                        mm.then_inc(f_h, 1)
                        if e >= 2:
                            second(n, e - 2, par)
                    elif s == "T":
                        second(n - 1, NE - 2, 1 - par)
                        second(n - 1, NE - 1, 1 - par)
                    elif s in ("aX0", "aX1"):
                        c = int(s[2])
                        pe.wait_ge(a_xn, 4 * b + 4)
                        wait(pe, (a_pl, a_ce)[c], NJ * b)
                        for t in range(NT):
                            mm = nc.tensor.transpose(ab[c][:, t * P:(t + 1) * P], xna[:, t, c * P:(c + 1) * P],
                                                     ident[:])
                        mm.then_inc(a_xt, 1)
                    elif s in ("aQ0", "aQ1"):
                        c = int(s[2])
                        for u in range(2):
                            if c == 0:
                                pe.wait_ge(a_xl, 2 * b + 2)
                            else:
                                pe.wait_ge(a_vl, 4 * b + 3 + u)
                            for k in range(KC):
                                mm = three(ab[u][:], wah[:, u, k, c * P:(c + 1) * P], wal[:, u, k, c * P:(c + 1) * P],
                                           axh[:, k, WIN:WIN + L], axl[:, k, WIN:WIN + L],
                                           start=(k == 0), stop=(k == KC - 1))
                            mm.then_inc(a_qk, 1)
                    elif s[:2] == "aV":
                        u = int(s[2])
                        if u < 2:
                            pe.wait_ge(a_qkl, 4 * b + u + 1)
                        else:
                            pe.wait_ge(a_vl, 4 * b + u - 1)
                        for w in (2 * u, 2 * u + 1):
                            ws = slice(WIN * w, WIN * w + P)
                            for k in range(KC):
                                mm = three(ab[u % 2][:, (w % 2) * D:(w % 2 + 1) * D], axh[:, k, ws], axl[:, k, ws],
                                           wah[:, 2, k, :], wal[:, 2, k, :], start=(k == 0), stop=(k == KC - 1))
                        mm.then_inc(a_v, 1)
                    elif s == "aO":
                        pe.wait_ge(a_cl, 2 * b + 2)
                        pe.wait_ge(a_m, 4 * NJ * (b + 1))
                        for t in range(NT):
                            ts = slice(WIN + t * P, WIN + (t + 1) * P)
                            for k in range(KC):
                                mm = three(sp_[:, t, :], axh[:, k, ts], axl[:, k, ts], wah[:, 3, k, :],
                                           wal[:, 3, k, :], start=(k == 0), stop=(k == KC - 1))
                        mm.then_inc(a_o, 1)
                    elif s[0] in "JK":
                        st = int(s[1:])
                        if scored(s):
                            j, w = st, st % NW
                            k0 = min(WIN * w, WIN + L - 2 * P)
                            if w == 0:
                                pe.wait_ge(a_stk, NSTK * (2 * b + j // NW + 1))
                            if j == 0:
                                wait(pe, a_x2, 2 * b)
                            else:
                                pe.wait_ge(a_m, 4 * (NJ * b + j))
                            if j == NW - 1:
                                pe.wait_ge(a_qw, 128 * b + 128)
                            for r in range(NP):
                                mm = nc.tensor.matmul(sp_[:, r, :], qs[:, r, w].rearrange("p h q -> p (h q)"),
                                                      ks[:, r, k0:k0 + 2 * P], start=True, stop=True)
                            mm.then_inc(a_s, 1)
                        if s[0] == "J" and 2 <= st <= NJ + 1:
                            j = st - 2
                            pe.wait_ge(a_pn, NJ * b + j + 1)
                            if j == 0:
                                pe.wait_ge(a_qkl, 4 * b + 3)
                            else:
                                pe.wait_ge(a_pl, NJ * b + j)
                            for r in range(NP):
                                mm = nc.tensor.transpose(ptb[:, r * P:(r + 1) * P], pr[:, j % 3, r, :], ident[:])
                            mm.then_inc(a_pt, 1)
                        if s[0] == "J" and 3 <= st <= NJ + 2:
                            j = st - 3
                            c, w = j // NW, j % NW
                            pe.wait_ge(a_ph, NJ * b + j + 1)
                            pe.wait_ge(a_pl, NJ * b + j + 1)
                            if j == 0:
                                pe.wait_ge(a_qkl, 4 * b + 4)
                                pe.wait_ge(a_vl, 4 * b + 4)
                            else:
                                pe.wait_ge(a_ce, NJ * b + j)
                            mm = three(cxb[:], vh[:, w, c * P:(c + 1) * P], vl[:, w, c * P:(c + 1) * P],
                                       pth[:, j % 2, :], ptl[:, j % 2, :], start=True, stop=True)
                            mm.then_inc(a_pv, 1)

            passes(pe, slot)


_INS = ["L0_attn_x", "L0_attn_Wq", "L0_attn_Wk", "L0_attn_Wv", "L0_attn_Wo", "L0_ffn_routing_W",
        "L0_ffn_expert_bias", "L0_ffn_sW1", "L0_ffn_sb1", "L0_ffn_sW2", "L0_ffn_sb2", "L0_ffn_rW1", "L0_ffn_rb1",
        "L0_ffn_rW2", "L0_ffn_rb2"]


def kernel(**inputs):
    import numpy as _np
    import concourse.bacc as _bacc
    from concourse.bass_utils import run_bass_kernel_spmd as _run

    nc = _bacc.Bacc("TRN2", target_bir_lowering=False, num_devices=1)
    arrays, args = {}, []
    for name in _INS:
        a = _np.ascontiguousarray(inputs[name])
        arrays[name + "_dram"] = a
        args.append(nc.dram_tensor(name + "_dram", a.shape, mybir.dt.from_np(a.dtype), kind="ExternalInput").ap())
    shape = arrays["L0_attn_x_dram"].shape
    args.append(nc.dram_tensor("out_dram", shape, F32, kind="ExternalOutput").ap())
    experts = arrays["L0_ffn_expert_bias_dram"].shape[0]
    args.append(nc.dram_tensor("gates_dram", (experts, shape[1]), F32, kind="Internal").ap())
    args.append(nc.dram_tensor("qk_dram", (2, 2, 2, 32, 4, shape[1]), F32, kind="Internal").ap())
    macaron_block(nc, *args)
    r = _run(nc, [arrays], core_ids=[0])
    return r.results[0]["out_dram"]
```
